# Optimizing a Trainium2 kernel written in Bass

```python
import numpy as np
import jax
import jax.numpy as jnp

def _softmax(x, axis=-1):
    return jax.nn.softmax(x, axis=axis)

def _gelu(x):
    return jax.nn.gelu(x, approximate=True)

def _silu(x):
    return jax.nn.silu(x)

def _sigmoid(x):
    return jax.nn.sigmoid(x)

def _layernorm(x, axis=-1, eps=1e-05):
    m = jnp.mean(x, axis=axis, keepdims=True)
    v = jnp.var(x, axis=axis, keepdims=True)
    return (x - m) / jnp.sqrt(v + eps)

def _scatter_add(tgt, idx, src, axis=0):
    return tgt.at[idx].add(src)

def _segment_sum(src, seg, n):
    return jax.ops.segment_sum(src, seg, n)
kernel_name = 'mk_dlrm_tower_d1_rec_r8_ebe3e4'

def setup_inputs(seed: int=0):
    np.random.seed(seed)
    _w = jnp.asarray

    def _rec_inputs():
        import jax
        import jax.numpy as jnp
        _tk = jax.random.key(seed)
        ids = jnp.stack([jax.random.randint(jax.random.fold_in(_tk, 200 + f), (2048,), 0, v, jnp.int32) for f, v in enumerate([125000, 1000, 12500, 1000, 1250, 12500, 1250, 12500, 1250, 1250, 1250, 12500, 1250, 1000, 12500, 1000, 1000, 12500, 1000, 1250, 12500, 12500, 1000, 1000, 1000, 1250])], axis=1)
        tbl_0 = 0.05 * jax.random.normal(jax.random.fold_in(_tk, 500 + 0), (125000, 128), jnp.float32)
        tbl_1 = 0.05 * jax.random.normal(jax.random.fold_in(_tk, 500 + 1), (1000, 128), jnp.float32)
        tbl_2 = 0.05 * jax.random.normal(jax.random.fold_in(_tk, 500 + 2), (12500, 128), jnp.float32)
        tbl_3 = 0.05 * jax.random.normal(jax.random.fold_in(_tk, 500 + 3), (1000, 128), jnp.float32)
        tbl_4 = 0.05 * jax.random.normal(jax.random.fold_in(_tk, 500 + 4), (1250, 128), jnp.float32)
        tbl_5 = 0.05 * jax.random.normal(jax.random.fold_in(_tk, 500 + 5), (12500, 128), jnp.float32)
        tbl_6 = 0.05 * jax.random.normal(jax.random.fold_in(_tk, 500 + 6), (1250, 128), jnp.float32)
        tbl_7 = 0.05 * jax.random.normal(jax.random.fold_in(_tk, 500 + 7), (12500, 128), jnp.float32)
        tbl_8 = 0.05 * jax.random.normal(jax.random.fold_in(_tk, 500 + 8), (1250, 128), jnp.float32)
        tbl_9 = 0.05 * jax.random.normal(jax.random.fold_in(_tk, 500 + 9), (1250, 128), jnp.float32)
        tbl_10 = 0.05 * jax.random.normal(jax.random.fold_in(_tk, 500 + 10), (1250, 128), jnp.float32)
        tbl_11 = 0.05 * jax.random.normal(jax.random.fold_in(_tk, 500 + 11), (12500, 128), jnp.float32)
        tbl_12 = 0.05 * jax.random.normal(jax.random.fold_in(_tk, 500 + 12), (1250, 128), jnp.float32)
        tbl_13 = 0.05 * jax.random.normal(jax.random.fold_in(_tk, 500 + 13), (1000, 128), jnp.float32)
        tbl_14 = 0.05 * jax.random.normal(jax.random.fold_in(_tk, 500 + 14), (12500, 128), jnp.float32)
        tbl_15 = 0.05 * jax.random.normal(jax.random.fold_in(_tk, 500 + 15), (1000, 128), jnp.float32)
        tbl_16 = 0.05 * jax.random.normal(jax.random.fold_in(_tk, 500 + 16), (1000, 128), jnp.float32)
        tbl_17 = 0.05 * jax.random.normal(jax.random.fold_in(_tk, 500 + 17), (12500, 128), jnp.float32)
        tbl_18 = 0.05 * jax.random.normal(jax.random.fold_in(_tk, 500 + 18), (1000, 128), jnp.float32)
        tbl_19 = 0.05 * jax.random.normal(jax.random.fold_in(_tk, 500 + 19), (1250, 128), jnp.float32)
        tbl_20 = 0.05 * jax.random.normal(jax.random.fold_in(_tk, 500 + 20), (12500, 128), jnp.float32)
        tbl_21 = 0.05 * jax.random.normal(jax.random.fold_in(_tk, 500 + 21), (12500, 128), jnp.float32)
        tbl_22 = 0.05 * jax.random.normal(jax.random.fold_in(_tk, 500 + 22), (1000, 128), jnp.float32)
        tbl_23 = 0.05 * jax.random.normal(jax.random.fold_in(_tk, 500 + 23), (1000, 128), jnp.float32)
        tbl_24 = 0.05 * jax.random.normal(jax.random.fold_in(_tk, 500 + 24), (1000, 128), jnp.float32)
        tbl_25 = 0.05 * jax.random.normal(jax.random.fold_in(_tk, 500 + 25), (1250, 128), jnp.float32)
        _rk = jax.random.fold_in(_tk, 7)
        r_dense_features = -0.000292821 + 1.00034 * jax.random.normal(jax.random.fold_in(_rk, 101), (2048, 128), jnp.float32)
        W_top1 = 0.0405887 * jax.random.normal(jax.random.fold_in(_tk, 801), (607, 512), jnp.float32)
        W_top2 = 0.0441942 * jax.random.normal(jax.random.fold_in(_tk, 802), (512, 256), jnp.float32)
        W_top3 = 0.0625 * jax.random.normal(jax.random.fold_in(_tk, 803), (256, 1), jnp.float32)
        b_top1 = jnp.zeros((512,), jnp.float32)
        b_top2 = jnp.zeros((256,), jnp.float32)
        return (r_dense_features, ids, tbl_0, tbl_1, tbl_2, tbl_3, tbl_4, tbl_5, tbl_6, tbl_7, tbl_8, tbl_9, tbl_10, tbl_11, tbl_12, tbl_13, tbl_14, tbl_15, tbl_16, tbl_17, tbl_18, tbl_19, tbl_20, tbl_21, tbl_22, tbl_23, tbl_24, tbl_25, W_top1, b_top1, W_top2, b_top2, W_top3)
    r_dense_features, ids, tbl_0, tbl_1, tbl_2, tbl_3, tbl_4, tbl_5, tbl_6, tbl_7, tbl_8, tbl_9, tbl_10, tbl_11, tbl_12, tbl_13, tbl_14, tbl_15, tbl_16, tbl_17, tbl_18, tbl_19, tbl_20, tbl_21, tbl_22, tbl_23, tbl_24, tbl_25, W_top1, b_top1, W_top2, b_top2, W_top3 = _rec_inputs()

    def _L0_rec_setup():
        import jax, jax.numpy as jnp
        import numpy as np
        F = 26
        _TRIU_I, _TRIU_J = np.triu_indices(F + 1, k=1)
        key = jax.random.key(seed)
        k1, k2 = jax.random.split(key)
        B, D = (4096, 128)
        dense_features = jax.random.normal(k1, (B, D), dtype=jnp.float32)
        sparse_features = jax.random.normal(k2, (B, F, D), dtype=jnp.float32)
        return {'dense_features': dense_features, 'sparse_features': sparse_features}
    _L0_rec_all = _L0_rec_setup()
    _L0_rec_in = {k: v for k, v in _L0_rec_all.items() if k in ()}
    del _L0_rec_all
    return {'r_dense_features': r_dense_features, 'ids': ids, 'tbl_0': tbl_0, 'tbl_1': tbl_1, 'tbl_2': tbl_2, 'tbl_3': tbl_3, 'tbl_4': tbl_4, 'tbl_5': tbl_5, 'tbl_6': tbl_6, 'tbl_7': tbl_7, 'tbl_8': tbl_8, 'tbl_9': tbl_9, 'tbl_10': tbl_10, 'tbl_11': tbl_11, 'tbl_12': tbl_12, 'tbl_13': tbl_13, 'tbl_14': tbl_14, 'tbl_15': tbl_15, 'tbl_16': tbl_16, 'tbl_17': tbl_17, 'tbl_18': tbl_18, 'tbl_19': tbl_19, 'tbl_20': tbl_20, 'tbl_21': tbl_21, 'tbl_22': tbl_22, 'tbl_23': tbl_23, 'tbl_24': tbl_24, 'tbl_25': tbl_25, 'W_top1': W_top1, 'b_top1': b_top1, 'W_top2': W_top2, 'b_top2': b_top2, 'W_top3': W_top3}

def reference(r_dense_features, ids, tbl_0, tbl_1, tbl_2, tbl_3, tbl_4, tbl_5, tbl_6, tbl_7, tbl_8, tbl_9, tbl_10, tbl_11, tbl_12, tbl_13, tbl_14, tbl_15, tbl_16, tbl_17, tbl_18, tbl_19, tbl_20, tbl_21, tbl_22, tbl_23, tbl_24, tbl_25, W_top1, b_top1, W_top2, b_top2, W_top3):
    import jax
    import jax.numpy as jnp

    def _L0_rec_ref(dense_features, sparse_features):
        import jax, jax.numpy as jnp
        import numpy as np
        F = 26
        _TRIU_I, _TRIU_J = np.triu_indices(F + 1, k=1)
        combined = jnp.concatenate([dense_features[:, None, :], sparse_features], axis=1)
        interactions = jnp.einsum('bfd,bgd->bfg', combined, combined)
        interactions_flat = interactions[:, _TRIU_I, _TRIU_J]
        return jnp.concatenate([dense_features, interactions_flat], axis=1)
    e = jnp.stack([tbl_0[ids[:, 0]], tbl_1[ids[:, 1]], tbl_2[ids[:, 2]], tbl_3[ids[:, 3]], tbl_4[ids[:, 4]], tbl_5[ids[:, 5]], tbl_6[ids[:, 6]], tbl_7[ids[:, 7]], tbl_8[ids[:, 8]], tbl_9[ids[:, 9]], tbl_10[ids[:, 10]], tbl_11[ids[:, 11]], tbl_12[ids[:, 12]], tbl_13[ids[:, 13]], tbl_14[ids[:, 14]], tbl_15[ids[:, 15]], tbl_16[ids[:, 16]], tbl_17[ids[:, 17]], tbl_18[ids[:, 18]], tbl_19[ids[:, 19]], tbl_20[ids[:, 20]], tbl_21[ids[:, 21]], tbl_22[ids[:, 22]], tbl_23[ids[:, 23]], tbl_24[ids[:, 24]], tbl_25[ids[:, 25]]], axis=1)
    z = _L0_rec_ref(r_dense_features, e)
    z = z.reshape(z.shape[0], -1)
    h = jnp.concatenate([z, r_dense_features], axis=1)
    h = jnp.maximum(h @ W_top1 + b_top1, 0.0)
    h = jnp.maximum(h @ W_top2 + b_top2, 0.0)
    y = h @ W_top3
    return y

_drawn_inputs = setup_inputs


def setup_inputs(seed=0):
    import zlib

    import numpy as np

    out = dict(_drawn_inputs(seed))
    spreads = {'b_top1': (0.0, 0.1), 'b_top2': (0.0, 0.1)}
    factors = {}
    for name, (base, spread) in spreads.items():
        noise = np.random.default_rng([zlib.crc32(name.encode()), seed]).standard_normal(out[name].shape)
        drawn = base * np.exp(spread * noise) if base else spread * noise
        out[name] = jnp.asarray(drawn.astype(out[name].dtype))
    for name, factor in factors.items():
        out[name] = (out[name] * factor).astype(out[name].dtype)
    return out
```

```python
from contextlib import ExitStack

import concourse.bass as bass
from concourse import mybir

P = 128
ALU = mybir.AluOpType
ACT = mybir.ActivationFunctionType
F32 = mybir.dt.float32


def dlrm_tower(nc, x, ids, tables, w_top1, b_top1, w_top2, b_top2, w_top3, out):
    batch, dim = x.shape
    n_tables = len(tables)
    feats = n_tables + 1
    hidden1, hidden2 = w_top2.shape
    pairs = feats * (feats - 1) // 2
    assert dim == P and feats <= 32 and w_top1.shape[0] == 2 * dim + pairs

    TILES = 4
    BLOCK = TILES * P
    BLOCKS = batch // BLOCK
    LANES = 4
    SLOT = P // LANES
    GCOLS = feats - 1
    QUADS = P // LANES
    FILL = 4
    TP_BANKS = -(-feats // FILL)
    GR_BANKS = QUADS // FILL
    COL_BANKS = -(-GCOLS // FILL)
    PAIR_CHUNKS = 3
    PCH = pairs // PAIR_CHUNKS
    assert PCH * PAIR_CHUNKS == pairs and PCH <= P
    N1, N2 = hidden1 // P, hidden2 // P
    PT_USES = COL_BANKS + PAIR_CHUNKS
    MM_USES = N1 + N2 + 1
    GATHERED = 16 * n_tables
    assert TP_BANKS * TILES % 2 == 0 and GR_BANKS % 2 == 0 and PT_USES % 2 == 0
    pair_at = [g * feats - g * (g + 1) // 2 for g in range(GCOLS)]

    with ExitStack() as ctx:
        def sb(name, shape, dt=F32):
            return ctx.enter_context(nc.sbuf_tensor(name, shape, dt))

        def bank(name):
            return ctx.enter_context(nc.psum_tensor(name, [P, 512], F32))

        def sem(name):
            return ctx.enter_context(nc.semaphore(name))

        index = [sb(f"index{s}", [P, n_tables], mybir.dt.int32) for s in range(2)]
        rows = [sb(f"rows{s}", [P, feats, P]) for s in range(2)]
        feat = sb("feat", [P, TILES, P, SLOT])
        x_next = sb("x_next", [P, LANES, P])
        x_cols = sb("x_cols", [P, LANES, P])
        gram = sb("gram", [P, GCOLS, P])
        packed = sb("packed", [P, LANES, pairs])
        pair_cols = sb("pair_cols", [P, PAIR_CHUNKS, BLOCK])
        h1 = sb("h1", [P, N1, BLOCK])
        h2 = sb("h2", [P, N2, BLOCK])
        y = sb("y", [P, LANES])
        w1x = sb("w1x", [P, hidden1])
        w1x_again = sb("w1x_again", [P, hidden1])
        w1x_sum = sb("w1x_sum", [P, hidden1])
        w1p = sb("w1p", [P, PAIR_CHUNKS, hidden1])
        w2 = sb("w2", [P, N1, hidden2])
        w3 = sb("w3", [P, N2])
        b1 = sb("b1", [P, N1])
        b2 = sb("b2", [P, N2])
        ident = sb("ident", [P, P])

        tp = [bank(f"tp{s}") for s in range(2)]
        gr = [bank(f"gr{s}") for s in range(2)]
        pt = [bank(f"pt{s}") for s in range(2)]
        mm = [bank(f"mm{s}") for s in range(2)]

        weights_landed = sem("weights_landed")
        w1x_summed = sem("w1x_summed")
        ident_zeroed = sem("ident_zeroed")
        ident_ready = sem("ident_ready")
        feat_padded = sem("feat_padded")
        index_landed = [sem(f"index_landed{s}") for s in range(2)]
        x_landed = [sem(f"x_landed{s}") for s in range(2)]
        rows_landed = [sem(f"rows_landed{s}") for s in range(2)]
        tp_full = sem("tp_full")
        tp_taken = sem("tp_taken")
        gr_full = sem("gr_full")
        gr_taken = sem("gr_taken")
        pt_full = sem("pt_full")
        pt_taken = sem("pt_taken")
        mm_full = sem("mm_full")
        mm_taken = sem("mm_taken")
        tile_begun = sem("tile_begun")
        x_committed = sem("x_committed")
        y_stored = sem("y_stored")
        WEIGHTS = 16 * 7

        block = ctx.enter_context(nc.Block())

        def peeled(eng, body):
            body(0)
            with eng.Fori(1, BLOCKS) as i:
                body(i)
            body(BLOCKS)

        def first(i):
            return isinstance(i, int) and i == 0

        def last(i):
            return isinstance(i, int) and i == BLOCKS

        @block.sync
        def _(sp):
            def load_tile(i, t):
                s, n = t % 2, 2 * i + t // 2
                if not (first(i) and t < 2):
                    sp.wait_ge(rows_landed[s], n * GATHERED)
                sp.dma_start(index[s][:], ids[bass.ds(i * BLOCK + t * P, P), :]).then_inc(index_landed[s], 16)
                if not (first(i) and t < 2):
                    sp.wait_ge(tp_full, TP_BANKS * (i * TILES + t - 1))
                sp.dma_start(rows[s][:, 0, :], x[bass.ds(i * BLOCK + t * P, P), :]).then_inc(x_landed[s], 16)

            def body(i):
                if last(i):
                    return
                for t in range(TILES):
                    load_tile(i, t)
                    if first(i) and t == 1:
                        load_weights()

            def load_weights():
                sp.dma_start(w1x[:], w_top1[0:P, :]).then_inc(weights_landed, 16)
                sp.dma_start(w1x_again[:], w_top1[P + pairs:2 * P + pairs, :]).then_inc(weights_landed, 16)
                sp.dma_start(w1p[0:PCH], w_top1[P:P + pairs, :].rearrange("(c p) n -> p c n", p=PCH)) \
                    .then_inc(weights_landed, 16)
                sp.dma_start(w2[:], w_top2.rearrange("(c p) n -> p c n", p=P)).then_inc(weights_landed, 16)
                with nc.allow_non_contiguous_dma(reason="a few hundred words, once"):
                    sp.dma_start(w3[:], w_top3.rearrange("(c p) o -> p (c o)", p=P)).then_inc(weights_landed, 16)
                    sp.dma_start(b1[:], b_top1.rearrange("(c p) -> p c", p=P)).then_inc(weights_landed, 16)
                    sp.dma_start(b2[:], b_top2.rearrange("(c p) -> p c", p=P)).then_inc(weights_landed, 16)

            peeled(sp, body)

        @block.gpsimd
        def _(pool):
            def body(i):
                if last(i):
                    return
                for t in range(TILES):
                    s, n = t % 2, 2 * i + t // 2
                    pool.wait_ge(index_landed[s], 16 * (n + 1))
                    if not (first(i) and t < 2):
                        pool.wait_ge(tp_full, TP_BANKS * (i * TILES + t - 1))
                    pool.sem_inc(tile_begun, 1)
                    for f in range(n_tables):
                        nc.gpsimd.indirect_dma_start(
                            rows[s][:, f + 1, :], None, tables[f][:, :],
                            bass.IndirectOffsetOnAxis(ap=index[s][:, f:f + 1], axis=0)).then_inc(rows_landed[s], 16)
                    if first(i) and t == 0:
                        nc.gpsimd.memset(ident[:], 0.0).then_inc(ident_zeroed, 1)
                        pool.wait_ge(ident_zeroed, 1)
                        nc.gpsimd.affine_select(out=ident[:], in_=ident[:], compare_op=ALU.not_equal, fill=1.0,
                                                base=0, pattern=[[-1, P]], channel_multiplier=1) \
                            .then_inc(ident_ready, 1)

            peeled(pool, body)

        @block.tensor
        def _(pe):
            def transpose_bank(i, t, k):
                n = TP_BANKS * (i * TILES + t) + k
                if k == 0:
                    pe.wait_ge(x_landed[t % 2], 16 * (2 * i + t // 2 + 1))
                    pe.wait_ge(rows_landed[t % 2], GATHERED * (2 * i + t // 2 + 1))
                if not (first(i) and t == 0 and k < 2):
                    pe.wait_ge(tp_taken, n - 1)
                for f in range(FILL * k, min(FILL * k + FILL, feats)):
                    at = (f - FILL * k) * P
                    ins = nc.tensor.transpose(tp[(TP_BANKS * t + k) % 2][:, at:at + P], rows[t % 2][:, f, :], ident[:])
                ins.then_inc(tp_full, 1)

            def gram_bank(i, t, k):
                n = GR_BANKS * (i * TILES + t) + k
                if k == 0:
                    pe.wait_ge(tp_taken, TP_BANKS * (i * TILES + t + 1))
                if not (first(i) and t == 0 and k < 2):
                    pe.wait_ge(gr_taken, n - 1)
                for q in range(FILL):
                    b = LANES * (FILL * k + q)
                    ins = nc.tensor.matmul(
                        gr[k % 2][:, q * LANES * GCOLS:(q + 1) * LANES * GCOLS],
                        feat[:, t, b:b + LANES, :].rearrange("d j f -> d (j f)"), feat[:, t, b:b + LANES, 0:GCOLS],
                        start=True, stop=True)
                ins.then_inc(gr_full, 1)

            def column_bank(i, k):
                if k == 0:
                    pe.wait_ge(gr_taken, GR_BANKS * TILES * (i + 1))
                if k >= 2:
                    pe.wait_ge(pt_taken, PT_USES * i + k - 1)
                for g in range(FILL * k, min(FILL * k + FILL, GCOLS)):
                    at = (g - FILL * k) * P
                    ins = nc.tensor.transpose(pt[k % 2][:, at:at + P], gram[:, g, :], ident[:])
                ins.then_inc(pt_full, 1)

            def pair_bank(i, c):
                k = COL_BANKS + c
                if c == 0:
                    pe.wait_ge(pt_taken, PT_USES * i + COL_BANKS)
                else:
                    pe.wait_ge(pt_taken, PT_USES * i + k - 1)
                for j in range(LANES):
                    ins = nc.tensor.transpose(pt[k % 2][0:PCH, j * P:(j + 1) * P],
                                              packed[:, j, c * PCH:(c + 1) * PCH], ident[:])
                ins.then_inc(pt_full, 1)

            def mm_bank(i, k):
                if k >= 2:
                    pe.wait_ge(mm_taken, MM_USES * i + k - 1)
                return mm[k % 2]

            def layer1(i, n):
                to = mm_bank(i, n)
                if n == 0:
                    pe.wait_ge(pt_taken, PT_USES * (i + 1))
                    pe.wait_ge(x_committed, i + 1)
                    if first(i):
                        pe.wait_ge(w1x_summed, 1)
                        pe.wait_ge(weights_landed, WEIGHTS)
                cols = slice(n * P, (n + 1) * P)
                nc.tensor.matmul(to[:], w1x_sum[:, cols], x_cols[:].rearrange("d j q -> d (j q)"),
                                 start=True, stop=False)
                for c in range(PAIR_CHUNKS):
                    ins = nc.tensor.matmul(to[:], w1p[0:PCH, c, cols], pair_cols[0:PCH, c, :],
                                           start=False, stop=(c == PAIR_CHUNKS - 1))
                ins.then_inc(mm_full, 1)

            def layer2(i, n):
                to = mm_bank(i, N1 + n)
                if n == 0:
                    pe.wait_ge(mm_taken, MM_USES * i + N1)
                for c in range(N1):
                    ins = nc.tensor.matmul(to[:], w2[:, c, n * P:(n + 1) * P], h1[:, c, :],
                                           start=(c == 0), stop=(c == N1 - 1))
                ins.then_inc(mm_full, 1)

            def layer3(i):
                to = mm_bank(i, N1 + N2)
                pe.wait_ge(mm_taken, MM_USES * i + N1 + N2)
                for j in range(LANES):
                    for c in range(N2):
                        ins = nc.tensor.matmul(to[:, j:j + 1], h2[:, c, j * P:(j + 1) * P], w3[:, c:c + 1],
                                               start=(c == 0), stop=(c == N2 - 1))
                ins.then_inc(mm_full, 1)

            def body(i):
                if first(i):
                    pe.wait_ge(ident_ready, 1)
                    pe.wait_ge(feat_padded, 1)
                for t in range(TILES):
                    if t == 1 and not first(i):
                        for k in range(COL_BANKS):
                            column_bank(i - 1, k)
                    for k in range(GR_BANKS):
                        if k < TP_BANKS and not last(i):
                            transpose_bank(i, t, k)
                        if t == 0 and not first(i):
                            gram_bank(i - 1, TILES - 1, k)
                        elif t > 0 and not last(i):
                            gram_bank(i, t - 1, k)
                    if t == 1 and not first(i):
                        for c in range(PAIR_CHUNKS):
                            pair_bank(i - 1, c)
                    if t == 2 and not first(i):
                        if last(i):
                            pe.wait_ge(mm_taken, MM_USES * (i - 1))
                        for n in range(N1):
                            layer1(i - 1, n)
                    if t == 3 and not first(i):
                        for n in range(N2):
                            layer2(i - 1, n)
                        layer3(i - 1)

            peeled(pe, body)

        @block.scalar
        def _(act):
            def take_features(i, t, k):
                n = TP_BANKS * (i * TILES + t) + k
                f0, f1 = FILL * k, min(FILL * k + FILL, feats)
                if k == 0 and not first(i):
                    act.wait_ge(gr_full, GR_BANKS * ((i - 1) * TILES + t + 1))
                    if t == 0:
                        act.wait_ge(x_committed, i)
                act.wait_ge(tp_full, n + 1)
                src = tp[(TP_BANKS * t + k) % 2]
                if k == 0:
                    nc.scalar.copy(x_next[:, :, t * QUADS:(t + 1) * QUADS],
                                   src[:, 0:P].rearrange("d (q j) -> d j q", j=LANES))
                nc.scalar.copy(feat[:, t, :, f0:f1].rearrange("d b f -> d f b"),
                               src[:, 0:(f1 - f0) * P].rearrange("d (f b) -> d f b", b=P)).then_inc(tp_taken, 1)

            def relu(i, k, to, bias):
                act.wait_ge(mm_full, MM_USES * i + k + 1)
                nc.scalar.activation(to, mm[k % 2][:], ACT.Relu, bias=bias).then_inc(mm_taken, 1)

            def body(i):
                if first(i):
                    act.wait_ge(weights_landed, WEIGHTS)
                for t in range(TILES):
                    if not last(i):
                        for k in range(TP_BANKS):
                            take_features(i, t, k)
                    if t == 2 and not first(i):
                        for n in range(N1):
                            relu(i - 1, n, h1[:, n, :], b1[:, n:n + 1])
                    if t == 3 and not first(i):
                        for n in range(N2):
                            relu(i - 1, N1 + n, h2[:, n, :], b2[:, n:n + 1])
                        act.wait_ge(mm_full, MM_USES * i)
                        nc.scalar.copy(y[:], mm[(N1 + N2) % 2][:, 0:LANES]).then_inc(mm_taken, 1)
                        act.wait_ge(mm_taken, MM_USES * i)
                        act.dma_start(out[bass.ds((i - 1) * BLOCK, BLOCK), :].rearrange("(q j) o -> q (j o)", j=LANES),
                                      y[:]).then_inc(y_stored, 16)
                        act.wait_ge(y_stored, 16 * i)

            peeled(act, body)

        @block.vector
        def _(dve):
            def take_gram(i, t, k):
                n = GR_BANKS * (i * TILES + t) + k
                dve.wait_ge(gr_full, n + 1)
                quad = t * QUADS + FILL * k
                for j in range(LANES):
                    part = slice(j * SLOT, (j + 1) * SLOT)
                    src = gr[k % 2][part, 0:FILL * LANES * GCOLS].rearrange("p (q j g) -> p q j g", q=FILL, j=LANES)
                    ins = nc.vector.tensor_copy(gram[part, :, quad:quad + FILL].rearrange("p g q -> p q g"),
                                                src[:, :, j, :])
                ins.then_inc(gr_taken, 1)

            def take_columns(i, k):
                dve.wait_ge(pt_full, PT_USES * i + k + 1)
                for g in range(FILL * k, min(FILL * k + FILL, GCOLS)):
                    at = (g - FILL * k) * P
                    src = pt[k % 2][:, at:at + P].rearrange("q (j f) -> q j f", j=LANES)
                    ins = nc.vector.tensor_copy(packed[:, :, pair_at[g]:pair_at[g] + feats - 1 - g],
                                                src[:, :, g + 1:feats])
                ins.then_inc(pt_taken, 1)

            def take_pairs(i, c):
                k = COL_BANKS + c
                dve.wait_ge(pt_full, PT_USES * i + k + 1)
                nc.vector.tensor_copy(pair_cols[0:PCH, c, :], pt[k % 2][0:PCH, :]).then_inc(pt_taken, 1)

            def body(i):
                if first(i):
                    nc.vector.memset(feat[:, :, :, feats:SLOT], 0.0).then_inc(feat_padded, 1)
                    dve.wait_ge(weights_landed, WEIGHTS)
                    nc.vector.tensor_tensor(w1x_sum[:], w1x[:], w1x_again[:], ALU.add).then_inc(w1x_summed, 1)
                for t in range(TILES):
                    if t == 1 and not first(i):
                        for k in range(COL_BANKS):
                            take_columns(i - 1, k)
                    for k in range(GR_BANKS):
                        if t == 0 and not first(i):
                            take_gram(i - 1, TILES - 1, k)
                        elif t > 0 and not last(i):
                            take_gram(i, t - 1, k)
                    if t == 1 and not first(i):
                        for c in range(PAIR_CHUNKS):
                            take_pairs(i - 1, c)
                if not last(i):
                    dve.wait_ge(tp_taken, TP_BANKS * (i * TILES + TILES - 1) + 1)
                    if not first(i):
                        dve.wait_ge(mm_full, MM_USES * (i - 1) + N1)
                    nc.vector.tensor_copy(x_cols[:], x_next[:]).then_inc(x_committed, 1)

            peeled(dve, body)


def kernel(**inputs):
    import numpy as _np
    import concourse.bacc as _bacc
    from concourse import mybir as _mybir
    from concourse.bass_utils import run_bass_kernel_spmd as _run

    nc = _bacc.Bacc("TRN2", target_bir_lowering=False, num_devices=1)
    arrays, dram = {}, {}
    for name, value in inputs.items():
        a = _np.ascontiguousarray(value)
        arrays[f"in_{name}"] = a
        dram[name] = nc.dram_tensor(f"in_{name}", a.shape, _mybir.dt.from_np(a.dtype), kind="ExternalInput").ap()
    tables = [dram[f"tbl_{n}"] for n in range(dram["ids"].shape[1])]
    batch = dram["ids"].shape[0]
    out = nc.dram_tensor("out_y", (batch, 1), _mybir.dt.float32, kind="ExternalOutput").ap()
    dlrm_tower(nc, dram["r_dense_features"], dram["ids"], tables, dram["W_top1"], dram["b_top1"],
               dram["W_top2"], dram["b_top2"], dram["W_top3"], out)
    r = _run(nc, [arrays], core_ids=[0])
    return r.results[0]["out_y"]
```

```python
from contextlib import ExitStack

import concourse.bass as bass
from concourse import mybir

P = 128
ALU = mybir.AluOpType
ACT = mybir.ActivationFunctionType
F32 = mybir.dt.float32
F32R = mybir.dt.float32r
F16 = mybir.dt.float16
I32 = mybir.dt.int32


def dlrm_tower(nc, x, ids, tables, w_top1, b_top1, w_top2, b_top2, w_top3, out):
    batch, dim = x.shape
    n_tables = len(tables)
    feats = n_tables + 1
    hidden1, hidden2 = w_top2.shape
    pairs = feats * (feats - 1) // 2
    assert dim == P and feats <= 32 and w_top1.shape[0] == 2 * dim + pairs

    HALVES = 2
    UNITS = 2
    TILES = HALVES * UNITS
    UNIT = HALVES * P
    BLOCK = TILES * P
    BLOCKS = batch // BLOCK
    LANES = 4
    SLOT = P // LANES
    GCOLS = feats - 1
    QUADS = P // LANES
    FILL = 4
    GR_BANKS = QUADS // FILL
    COL_BANKS = -(-GCOLS // FILL)
    PAIR_CHUNKS = 3
    PCH = pairs // PAIR_CHUNKS
    assert PCH * PAIR_CHUNKS == pairs and PCH <= P
    N1, N2 = hidden1 // P, hidden2 // P
    pair_at = [g * feats - g * (g + 1) // 2 for g in range(GCOLS)]

    HOT = 8
    hot = sorted(sorted(range(n_tables), key=lambda f: (tables[f].shape[0], -f))[:HOT])
    cold = [f for f in range(n_tables) if f not in hot]
    DUOS = HOT // 2
    VOCAB = tables[hot[0]].shape[0]
    CHUNKS = -(-VOCAB // P)
    VP = VOCAB // CHUNKS
    assert VP * CHUNKS == VOCAB and VOCAB <= 2048 and all(tables[f].shape[0] == VOCAB for f in hot)
    in_rows = [0] + [f + 1 for f in cold]
    ROW_BANKS = -(-len(in_rows) // FILL)

    TP = DUOS + HALVES * ROW_BANKS
    GR = HALVES * GR_BANKS
    GATHERED = 16 * len(cold)
    PT = COL_BANKS + PAIR_CHUNKS
    MM = N1 + N2 + 1
    RING = 4
    AHEAD = RING - 1
    STEPS = DUOS * CHUNKS
    assert TP % 2 == 0 and GR % 2 == 0 and STEPS % RING == 0

    def plan(first, last, u):
        ids_, rows_, hots = [], [], []
        if not last:
            ids_ = [("ids", d, 0) for d in range(DUOS)]
            rows_ = [("rows", h, k) for h in range(HALVES) for k in range(ROW_BANKS)]
            hots = [("hot", d, c) for d in range(DUOS) for c in range(CHUNKS)]
        grams = [("gram", h, k) for h in range(HALVES) for k in range(GR_BANKS)]
        steps = []

        def some(of, n):
            for _ in range(min(n, len(of))):
                steps.append(of.pop(0))

        mlp = []
        if u == 1 and not first:
            for k in range(COL_BANKS):
                steps.append(("columns", k, 0))
                some(ids_, 1)
                if k >= 2:
                    some(hots, 1)
            steps += [("pairs", c, 0) for c in range(PAIR_CHUNKS)]
            mlp = [("layer1", n, 0) for n in range(N1)] + [("layer2", n, 0) for n in range(N2)] + [("layer3", 0, 0)]
        if (u == 0 and first) or (u == 1 and last):
            grams = []
        for s in range(GR):
            some(ids_, 2)
            some(grams, 1)
            some(hots, -(-len(hots) // (GR - s)) if s >= 2 or not ids_ else 0)
            if s in (1, 2, 3, 4, 5) or s in (11, 12, 13, 14, 15):
                some(rows_, 1)
            if s % 2 == 0 and s >= 2:
                some(mlp, 1)
        some(rows_, len(rows_))
        some(mlp, len(mlp))
        return steps

    def runs(features):
        found, at = [], 0
        while at < len(features):
            n = 1
            while at + n < len(features) and features[at + n] - features[at + n - 1] == features[at + min(1, n)] - features[at]:
                n += 1
            found.append((at, features[at], features[at + 1] - features[at] if n > 1 else 1, n))
            at += n
        return found

    with ExitStack() as ctx:
        def sb(name, shape, dt=F32):
            return ctx.enter_context(nc.sbuf_tensor(name, shape, dt))

        def banks(name):
            return [ctx.enter_context(nc.psum_tensor(f"{name}{s}", [P, 512], F32)) for s in range(2)]

        def sem(name):
            return ctx.enter_context(nc.semaphore(name))

        index = [sb(f"index{s}", [P, n_tables], I32) for s in range(HALVES)]
        hot_index = sb("hot_index", [P, HALVES, n_tables], I32)
        hot_ids = sb("hot_ids", [P, HALVES, n_tables])
        ids_cols = sb("ids_cols", [P, DUOS, 2 * UNIT], F16)
        onehot = sb("onehot", [P, RING, 2 * UNIT], F32R)
        row_of = sb("row_of", [P, CHUNKS])
        row_of_int = sb("row_of_int", [P, CHUNKS], I32)
        high = sb("high", [P, HOT, CHUNKS, P], F32R)
        low = sb("low", [P, HOT, CHUNKS, P], F32R)
        rows = [sb(f"rows{s}", [P, len(in_rows), P]) for s in range(HALVES)]
        feat = sb("feat", [P, TILES, P, SLOT])
        x_cols = sb("x_cols", [P, LANES, P])
        gram = sb("gram", [P, GCOLS, P])
        packed = sb("packed", [P, LANES, pairs])
        pair_cols = sb("pair_cols", [P, PAIR_CHUNKS, BLOCK])
        h1 = sb("h1", [P, N1, BLOCK])
        h2 = packed[:].rearrange("q j p -> q (j p)")[:, 0:N2 * BLOCK].rearrange("p (c b) -> p c b", c=N2)
        y = sb("y", [P, LANES])
        w1x_sum = sb("w1x_sum", [P, hidden1])
        w1p = sb("w1p", [P, PAIR_CHUNKS, hidden1])
        w2 = sb("w2", [P, N1, hidden2])
        w3 = sb("w3", [P, N2])
        b1 = sb("b1", [P, N1])
        b2 = sb("b2", [P, N2])
        ident = sb("ident", [P, P])
        raw = [h1[:, 2 * s:2 * s + 2, :].rearrange("p n b -> p (n b)").rearrange("p (c d) -> p c d", d=P)
               for s in range(2)]
        w1x, w1x_again = pair_cols[:, 0, :], pair_cols[:, 1, :]

        tp = banks("tp")
        ht = banks("ht")
        gr = banks("gr")
        cm = banks("cm")

        weights_landed = sem("weights_landed")
        raw_landed = [sem(f"raw_landed{s}") for s in range(2)]
        high_ready = sem("high_ready")
        low_ready = sem("low_ready")
        w1x_summed = sem("w1x_summed")
        ident_zeroed = sem("ident_zeroed")
        ident_ready = sem("ident_ready")
        row_of_made = sem("row_of_made")
        row_of_ready = sem("row_of_ready")
        feat_padded = sem("feat_padded")
        index_landed = [sem(f"index_landed{s}") for s in range(HALVES)]
        hot_index_landed = sem("hot_index_landed")
        x_landed = [sem(f"x_landed{s}") for s in range(HALVES)]
        rows_landed = [sem(f"rows_landed{s}") for s in range(HALVES)]
        hot_ids_ready = sem("hot_ids_ready")
        tp_full = sem("tp_full")
        tp_taken = sem("tp_taken")
        onehot_ready = sem("onehot_ready")
        onehot_used = sem("onehot_used")
        ht_taken = sem("ht_taken")
        gr_full = sem("gr_full")
        gr0_taken = sem("gr0_taken")
        gr1_taken = sem("gr1_taken")
        pt_full = sem("pt_full")
        pt_taken = sem("pt_taken")
        mm_full = sem("mm_full")
        mm_taken = sem("mm_taken")
        tile_begun = sem("tile_begun")
        x_committed = sem("x_committed")
        y_stored = sem("y_stored")
        WEIGHTS = 16 * 7

        block = ctx.enter_context(nc.Block())

        def peeled(eng, body):
            body(0)
            with eng.Fori(1, BLOCKS) as i:
                body(i)
            body(BLOCKS)

        def first(i):
            return isinstance(i, int) and i == 0

        def last(i):
            return isinstance(i, int) and i == BLOCKS

        @block.sync
        def _(sp):
            def load_unit(i, u):
                n = UNITS * i + u
                start = i * BLOCK + u * UNIT
                for h in range(HALVES):
                    if not (first(i) and u == 0):
                        sp.wait_ge(rows_landed[h], GATHERED * n)
                    sp.dma_start(index[h][:], ids[bass.ds(start + h * P, P), :]).then_inc(index_landed[h], 16)
                    if h == 0:
                        if not (first(i) and u == 0):
                            sp.wait_ge(hot_ids_ready, n)
                        sp.dma_start(hot_index[:], ids[bass.ds(start, UNIT), :].rearrange("(h p) f -> p h f", p=P)) \
                            .then_inc(hot_index_landed, 16)
                    if not (first(i) and u == 0):
                        sp.wait_ge(tp_full, TP * (n - 1) + DUOS + ROW_BANKS * (h + 1))
                    sp.dma_start(rows[h][:, 0, :], x[bass.ds(start + h * P, P), :]).then_inc(x_landed[h], 16)

            def load_raw(t):
                s = t % 2
                if t >= 2:
                    sp.wait_ge(low_ready, t - 1)
                sp.dma_start(raw[s][0:VP], tables[hot[t]].rearrange("(p c) d -> p c d", c=CHUNKS)) \
                    .then_inc(raw_landed[s], 16)

            def load_weights():
                sp.dma_start(w1x, w_top1[0:P, :]).then_inc(weights_landed, 16)
                sp.dma_start(w1x_again, w_top1[P + pairs:2 * P + pairs, :]).then_inc(weights_landed, 16)
                sp.dma_start(w1p[0:PCH], w_top1[P:P + pairs, :].rearrange("(c p) n -> p c n", p=PCH)) \
                    .then_inc(weights_landed, 16)
                sp.dma_start(w2[:], w_top2.rearrange("(c p) n -> p c n", p=P)).then_inc(weights_landed, 16)
                with nc.allow_non_contiguous_dma(reason="a few hundred words, once"):
                    sp.dma_start(w3[:], w_top3.rearrange("(c p) o -> p (c o)", p=P)).then_inc(weights_landed, 16)
                    sp.dma_start(b1[:], b_top1.rearrange("(c p) -> p c", p=P)).then_inc(weights_landed, 16)
                    sp.dma_start(b2[:], b_top2.rearrange("(c p) -> p c", p=P)).then_inc(weights_landed, 16)

            def body(i):
                if last(i):
                    return
                for u in range(UNITS):
                    load_unit(i, u)
                    if first(i) and u == 0:
                        for t in range(HOT):
                            load_raw(t)
                        load_weights()

            peeled(sp, body)

        @block.gpsimd
        def _(pool):
            def constants():
                nc.gpsimd.memset(ident[:], 0.0).then_inc(ident_zeroed, 1)
                pool.wait_ge(ident_zeroed, 1)
                nc.gpsimd.affine_select(out=ident[:], in_=ident[:], compare_op=ALU.not_equal, fill=1.0, base=0,
                                        pattern=[[-1, P]], channel_multiplier=1).then_inc(ident_ready, 1)
                nc.gpsimd.iota(row_of_int[:], pattern=[[1, CHUNKS]], base=0, channel_multiplier=CHUNKS) \
                    .then_inc(row_of_made, 1)

            def body(i):
                if first(i):
                    constants()
                if last(i):
                    return
                for u in range(UNITS):
                    n = UNITS * i + u
                    for h in range(HALVES):
                        pool.wait_ge(index_landed[h], 16 * (n + 1))
                        if not (first(i) and u == 0):
                            pool.wait_ge(tp_full, TP * (n - 1) + DUOS + ROW_BANKS * (h + 1))
                        pool.sem_inc(tile_begun, 1)
                        for k, f in enumerate(cold):
                            nc.gpsimd.indirect_dma_start(
                                rows[h][:, k + 1, :], None, tables[f][:, :],
                                bass.IndirectOffsetOnAxis(ap=index[h][:, f:f + 1], axis=0)) \
                                .then_inc(rows_landed[h], 16)

            peeled(pool, body)

        @block.tensor
        def _(pe):
            def tp_bank(i, n, k):
                if not (first(i) and isinstance(n, int) and n == 0 and k < 2):
                    pe.wait_ge(tp_taken, TP * n + k - 1)
                return tp[k % 2]

            def spread_ids(i, n, d):
                if d == 0:
                    pe.wait_ge(hot_ids_ready, n + 1)
                to = tp_bank(i, n, d)
                for e in range(2):
                    for h in range(HALVES):
                        at = (e * HALVES + h) * P
                        f = hot[2 * d + e]
                        ins = nc.tensor.transpose(to[:, at:at + P], hot_ids[:, h, f:f + 1].to_broadcast([P, P]), ident[:])
                ins.then_inc(tp_full, 1)

            def turn_rows(i, n, h, k):
                if k == 0:
                    pe.wait_ge(x_landed[h], 16 * (n + 1))
                    pe.wait_ge(rows_landed[h], GATHERED * (n + 1))
                to = tp_bank(i, n, DUOS + ROW_BANKS * h + k)
                for r in range(FILL * k, min(FILL * k + FILL, len(in_rows))):
                    at = (r - FILL * k) * P
                    ins = nc.tensor.transpose(to[:, at:at + P], rows[h][:, r, :], ident[:])
                ins.then_inc(tp_full, 1)

            def look_up(i, n, d, c):
                if c == 0 and not (first(i) and isinstance(n, int) and n == 0 and d < 2):
                    pe.wait_ge(ht_taken, DUOS * n + d - 1)
                if c == 0 and first(i) and isinstance(n, int) and n == 0:
                    pe.wait_ge(low_ready, 2 * d + 2)
                pe.wait_ge(onehot_ready, STEPS * n + CHUNKS * d + c + 1)
                for e in range(2):
                    t = 2 * d + e
                    to = ht[d % 2][:, e * UNIT:(e + 1) * UNIT]
                    moving = onehot[0:VP, (CHUNKS * d + c) % RING, e * UNIT:(e + 1) * UNIT]
                    nc.tensor.matmul(to, high[0:VP, t, c, :], moving, start=(c == 0 and e == 0), stop=False,
                                     skip_group_check=True)
                    ins = nc.tensor.matmul(to, low[0:VP, t, c, :], moving, start=False, stop=(c == CHUNKS - 1),
                                           skip_group_check=True)
                ins.then_inc(onehot_used, 1)

            def gram_bank(i, u, h, k):
                n = UNITS * i + u
                if h == 0 and k == 0:
                    pe.wait_ge(tp_taken, TP * (n + 1))
                    pe.wait_ge(ht_taken, DUOS * (n + 1))
                m = GR * n + GR_BANKS * h + k
                if not (first(i) and u == 0 and h == 0 and k < 2):
                    pe.wait_ge((gr0_taken, gr1_taken)[k % 2], GR // 2 * n + (GR_BANKS * h + k) // 2)
                for q in range(FILL):
                    b = LANES * (FILL * k + q)
                    items = feat[:, HALVES * u + h, b:b + LANES, :]
                    ins = nc.tensor.matmul(gr[k % 2][:, q * LANES * GCOLS:(q + 1) * LANES * GCOLS],
                                           items.rearrange("d j f -> d (j f)"), items[:, :, 0:GCOLS],
                                           start=True, stop=True)
                ins.then_inc(gr_full, 1)

            def turn_columns(i, k):
                if k == 0:
                    pe.wait_ge(gr0_taken, GR // 2 * UNITS * (i + 1))
                    pe.wait_ge(gr1_taken, GR // 2 * UNITS * (i + 1))
                if k >= 2:
                    pe.wait_ge(pt_taken, PT * i + k - 1)
                for g in range(FILL * k, min(FILL * k + FILL, GCOLS)):
                    at = (g - FILL * k) * P
                    ins = nc.tensor.transpose(cm[k % 2][:, at:at + P], gram[:, g, :], ident[:])
                ins.then_inc(pt_full, 1)

            def turn_pairs(i, c):
                k = COL_BANKS + c
                if c == 0:
                    pe.wait_ge(pt_taken, PT * i + COL_BANKS)
                else:
                    pe.wait_ge(pt_taken, PT * i + k - 1)
                for j in range(LANES):
                    ins = nc.tensor.transpose(cm[k % 2][0:PCH, j * P:(j + 1) * P],
                                              packed[:, j, c * PCH:(c + 1) * PCH], ident[:])
                ins.then_inc(pt_full, 1)

            def mm_bank(i, k):
                if k == 0:
                    pe.wait_ge(pt_taken, PT * (i + 1))
                elif k >= 2:
                    pe.wait_ge(mm_taken, MM * i + k - 1)
                return cm[(PT + k) % 2]

            def layer1(i, n):
                to = mm_bank(i, n)
                if n == 0:
                    pe.wait_ge(x_committed, i + 1)
                    pe.wait_ge(w1x_summed, 1)
                    pe.wait_ge(weights_landed, WEIGHTS)
                cols = slice(n * P, (n + 1) * P)
                nc.tensor.matmul(to[:], w1x_sum[:, cols], x_cols[:].rearrange("d j q -> d (j q)"),
                                 start=True, stop=False)
                for c in range(PAIR_CHUNKS):
                    ins = nc.tensor.matmul(to[:], w1p[0:PCH, c, cols], pair_cols[0:PCH, c, :],
                                           start=False, stop=(c == PAIR_CHUNKS - 1))
                ins.then_inc(mm_full, 1)

            def layer2(i, n):
                to = mm_bank(i, N1 + n)
                if n == 0:
                    pe.wait_ge(mm_taken, MM * i + N1)
                for c in range(N1):
                    ins = nc.tensor.matmul(to[:], w2[:, c, n * P:(n + 1) * P], h1[:, c, :],
                                           start=(c == 0), stop=(c == N1 - 1))
                ins.then_inc(mm_full, 1)

            def layer3(i):
                to = mm_bank(i, N1 + N2)
                pe.wait_ge(mm_taken, MM * i + N1 + N2)
                for j in range(LANES):
                    for c in range(N2):
                        ins = nc.tensor.matmul(to[:, j:j + 1], h2[:, c, j * P:(j + 1) * P], w3[:, c:c + 1],
                                               start=(c == 0), stop=(c == N2 - 1))
                ins.then_inc(mm_full, 1)

            def body(i):
                if first(i):
                    pe.wait_ge(ident_ready, 1)
                    pe.wait_ge(feat_padded, 1)
                for u in range(UNITS):
                    n = UNITS * i + u
                    for what, a, b in plan(first(i), last(i), u):
                        if what == "ids":
                            spread_ids(i, n, a)
                        elif what == "rows":
                            turn_rows(i, n, a, b)
                        elif what == "hot":
                            look_up(i, n, a, b)
                        elif what == "gram":
                            gram_bank(i - (u == 0), (u + 1) % UNITS, a, b)
                        elif what == "columns":
                            turn_columns(i - 1, a)
                        elif what == "pairs":
                            turn_pairs(i - 1, a)
                        elif what == "layer1":
                            layer1(i - 1, a)
                        elif what == "layer2":
                            layer2(i - 1, a)
                        elif what == "layer3":
                            layer3(i - 1)

            peeled(pe, body)

        @block.scalar
        def _(act):
            def cast_ids(i, n):
                act.wait_ge(hot_index_landed, 16 * (n + 1))
                nc.scalar.copy(hot_ids[:], hot_index[:]).then_inc(hot_ids_ready, 1)

            def take_high(d):
                for t in (2 * d, 2 * d + 1):
                    act.wait_ge(raw_landed[t % 2], 16 * (t // 2 + 1))
                    nc.scalar.copy(high[0:VP, t], raw[t % 2][0:VP]).then_inc(high_ready, 1)

            def take_ids(i, n, d):
                act.wait_ge(tp_full, TP * n + d + 1)
                if d == 0 and not (first(i) and isinstance(n, int) and n == 0):
                    act.wait_ge(onehot_ready, STEPS * n)
                nc.scalar.copy(ids_cols[:, d, :], tp[d % 2][:]).then_inc(tp_taken, 1)

            def take_rows(i, u, h, k):
                n = UNITS * i + u
                m = DUOS + ROW_BANKS * h + k
                t = HALVES * u + h
                features = in_rows[FILL * k:FILL * k + FILL]
                act.wait_ge(tp_full, TP * n + m + 1)
                src = tp[m % 2]
                if k == 0:
                    if t == 0 and not first(i):
                        act.wait_ge(x_committed, i)
                    if h == 0 and not first(i):
                        act.wait_ge(gr_full, GR * (n - 1))
                for at, f, step, count in runs(features):
                    to = feat[:, t, :, f:f + step * (count - 1) + 1:step]
                    ins = nc.scalar.copy(to.rearrange("d b f -> d f b"),
                                         src[:, at * P:(at + count) * P].rearrange("d (f b) -> d f b", b=P))
                ins.then_inc(tp_taken, 1)

            def take_looked_up(i, u, d):
                n = UNITS * i + u
                act.wait_ge(onehot_used, STEPS * n + CHUNKS * (d + 1))
                if d == 0 and not first(i):
                    act.wait_ge(gr_full, GR * (n - 1))
                a, b = hot[2 * d] + 1, hot[2 * d + 1] + 1
                for h in range(HALVES):
                    ins = nc.scalar.copy(feat[:, HALVES * u + h, :, a:b + 1:b - a].rearrange("d b e -> d e b"),
                                         ht[d % 2][:].rearrange("d (e h b) -> d e h b", e=2, h=HALVES)[:, :, h, :])
                ins.then_inc(ht_taken, 1)

            def take_gram(i, u, h, k):
                act.wait_ge(gr_full, GR * (UNITS * i + u) + GR_BANKS * h + k + 1)
                quad = (HALVES * u + h) * QUADS + FILL * k
                for j in range(LANES):
                    part = slice(j * SLOT, (j + 1) * SLOT)
                    src = gr[k % 2][part, 0:FILL * LANES * GCOLS].rearrange("p (q j g) -> p q j g", q=FILL, j=LANES)
                    ins = nc.scalar.copy(gram[part, :, quad:quad + FILL].rearrange("p g q -> p q g"), src[:, :, j, :])
                ins.then_inc(gr1_taken, 1)

            def relu(i, k, to, bias):
                act.wait_ge(mm_full, MM * i + k + 1)
                nc.scalar.activation(to, cm[(PT + k) % 2][:], ACT.Relu, bias=bias).then_inc(mm_taken, 1)

            def give_y(i):
                act.wait_ge(mm_full, MM * (i + 1))
                nc.scalar.copy(y[:], cm[(PT + N1 + N2) % 2][:, 0:LANES]).then_inc(mm_taken, 1)
                act.wait_ge(mm_taken, MM * (i + 1))
                act.dma_start(out[bass.ds(i * BLOCK, BLOCK), :].rearrange("(q j) o -> q (j o)", j=LANES),
                              y[:]).then_inc(y_stored, 16)

            def body(i):
                if first(i):
                    take_high(0)
                    cast_ids(i, 0)
                for u in range(UNITS):
                    n = UNITS * i + u
                    if not last(i) and not (first(i) and u == 0):
                        cast_ids(i, n)
                    for what, a, b in plan(first(i), last(i), u):
                        if what == "ids":
                            take_ids(i, n, a)
                        elif what == "rows":
                            take_rows(i, u, a, b)
                        elif what == "hot" and b == 0 and first(i) and u == 0 and a + 1 < DUOS:
                            take_high(a + 1)
                        elif what == "hot" and b == CHUNKS - 1:
                            take_looked_up(i, u, a)
                        elif what == "gram" and b % 2 == 1:
                            take_gram(i - (u == 0), (u + 1) % UNITS, a, b)
                        elif what == "layer1":
                            relu(i - 1, a, h1[:, a, :], b1[:, a:a + 1])
                        elif what == "layer2":
                            relu(i - 1, N1 + a, h2[:, a, :], b2[:, a:a + 1])
                        elif what == "layer3":
                            give_y(i - 1)
                    if u == UNITS - 1 and not first(i):
                        act.wait_ge(y_stored, 16 * i)

            peeled(act, body)

        @block.vector
        def _(dve):
            def take_low(d):
                for t in (2 * d, 2 * d + 1):
                    dve.wait_ge(high_ready, t + 1)
                    nc.vector.tensor_tensor(low[0:VP, t], raw[t % 2][0:VP], high[0:VP, t].bitcast(F32),
                                            ALU.subtract).then_inc(low_ready, 1)

            def make_onehot(i, n, m):
                d, c = divmod(m, CHUNKS)
                if c == 0:
                    dve.wait_ge(tp_taken, TP * n + d + 1)
                if not (first(i) and isinstance(n, int) and n == 0 and m < RING):
                    dve.wait_ge(onehot_used, STEPS * n + m - RING + 1)
                nc.vector.tensor_scalar(onehot[0:VP, m % RING, :], ids_cols[0:VP, d, :], row_of[0:VP, c:c + 1], None,
                                        ALU.is_equal).then_inc(onehot_ready, 1)

            def take_gram(i, u, h, k):
                dve.wait_ge(gr_full, GR * (UNITS * i + u) + GR_BANKS * h + k + 1)
                quad = (HALVES * u + h) * QUADS + FILL * k
                for j in range(LANES):
                    part = slice(j * SLOT, (j + 1) * SLOT)
                    src = gr[k % 2][part, 0:FILL * LANES * GCOLS].rearrange("p (q j g) -> p q j g", q=FILL, j=LANES)
                    ins = nc.vector.tensor_copy(gram[part, :, quad:quad + FILL].rearrange("p g q -> p q g"),
                                                src[:, :, j, :])
                ins.then_inc(gr0_taken, 1)

            def take_columns(i, k):
                dve.wait_ge(pt_full, PT * i + k + 1)
                for g in range(FILL * k, min(FILL * k + FILL, GCOLS)):
                    at = (g - FILL * k) * P
                    src = cm[k % 2][:, at:at + P].rearrange("q (j f) -> q j f", j=LANES)
                    ins = nc.vector.tensor_copy(packed[:, :, pair_at[g]:pair_at[g] + feats - 1 - g],
                                                src[:, :, g + 1:feats])
                ins.then_inc(pt_taken, 1)

            def take_pairs(i, c):
                k = COL_BANKS + c
                dve.wait_ge(pt_full, PT * i + k + 1)
                nc.vector.tensor_copy(pair_cols[0:PCH, c, :], cm[k % 2][0:PCH, :]).then_inc(pt_taken, 1)

            def body(i):
                if first(i):
                    nc.vector.memset(feat[:, :, :, feats:SLOT], 0.0).then_inc(feat_padded, 1)
                    dve.wait_ge(row_of_made, 1)
                    nc.vector.tensor_copy(row_of[:], row_of_int[:]).then_inc(row_of_ready, 1)
                    dve.wait_ge(row_of_ready, 1)
                    take_low(0)
                for u in range(UNITS):
                    n = UNITS * i + u
                    for what, a, b in plan(first(i), last(i), u):
                        if what == "hot":
                            m = CHUNKS * a + b
                            if first(i) and u == 0 and b == CHUNKS // 2 and a + 1 < DUOS:
                                take_low(a + 1)
                            for ahead in range(0 if m == 0 else AHEAD, AHEAD + 1):
                                if m + ahead < STEPS:
                                    make_onehot(i, n, m + ahead)
                        elif what == "gram" and b % 2 == 0:
                            take_gram(i - (u == 0), (u + 1) % UNITS, a, b)
                        elif what == "columns":
                            take_columns(i - 1, a)
                        elif what == "pairs":
                            take_pairs(i - 1, a)
                if first(i):
                    dve.wait_ge(weights_landed, WEIGHTS)
                    nc.vector.tensor_tensor(w1x_sum[:], w1x, w1x_again, ALU.add).then_inc(w1x_summed, 1)
                    dve.wait_ge(w1x_summed, 1)
                if not last(i):
                    dve.wait_ge(tp_taken, TP * (UNITS * (i + 1) - 1) + DUOS + ROW_BANKS * (HALVES - 1) + 1)
                    if not first(i):
                        dve.wait_ge(mm_full, MM * (i - 1) + N1)
                    nc.vector.tensor_copy(x_cols[:].rearrange("d j (t q) -> d t q j", t=TILES),
                                          feat[:, :, :, 0].rearrange("d t (q j) -> d t q j", j=LANES)) \
                        .then_inc(x_committed, 1)

            peeled(dve, body)


def kernel(**inputs):
    import numpy as _np
    import concourse.bacc as _bacc
    from concourse import mybir as _mybir
    from concourse.bass_utils import run_bass_kernel_spmd as _run

    nc = _bacc.Bacc("TRN2", target_bir_lowering=False, num_devices=1)
    arrays, dram = {}, {}
    for name, value in inputs.items():
        a = _np.ascontiguousarray(value)
        arrays[f"in_{name}"] = a
        dram[name] = nc.dram_tensor(f"in_{name}", a.shape, _mybir.dt.from_np(a.dtype), kind="ExternalInput").ap()
    tables = [dram[f"tbl_{n}"] for n in range(dram["ids"].shape[1])]
    batch = dram["ids"].shape[0]
    out = nc.dram_tensor("out_y", (batch, 1), _mybir.dt.float32, kind="ExternalOutput").ap()
    dlrm_tower(nc, dram["r_dense_features"], dram["ids"], tables, dram["W_top1"], dram["b_top1"],
               dram["W_top2"], dram["b_top2"], dram["W_top3"], out)
    r = _run(nc, [arrays], core_ids=[0])
    return r.results[0]["out_y"]
```

```python
from contextlib import ExitStack

import concourse.bass as bass
from concourse import mybir

P = 128
ALU = mybir.AluOpType
ACT = mybir.ActivationFunctionType
F32 = mybir.dt.float32
F32R = mybir.dt.float32r
F16 = mybir.dt.float16
I32 = mybir.dt.int32


def dlrm_tower(nc, x, ids, tables, w_top1, b_top1, w_top2, b_top2, w_top3, out):
    batch, dim = x.shape
    n_tables = len(tables)
    feats = n_tables + 1
    hidden1, hidden2 = w_top2.shape
    pairs = feats * (feats - 1) // 2
    assert dim == P and feats <= 32 and w_top1.shape[0] == 2 * dim + pairs

    HALVES = 2
    UNITS = 2
    TILES = HALVES * UNITS
    UNIT = HALVES * P
    BLOCK = TILES * P
    BLOCKS = batch // BLOCK
    LANES = 4
    SLOT = P // LANES
    GCOLS = feats - 1
    QUADS = P // LANES
    FILL = 4
    GR_BANKS = QUADS // FILL
    COL_BANKS = -(-GCOLS // FILL)
    PAIR_CHUNKS = 3
    PCH = pairs // PAIR_CHUNKS
    assert PCH * PAIR_CHUNKS == pairs and PCH <= P
    N1, N2 = hidden1 // P, hidden2 // P
    pair_at = [g * feats - g * (g + 1) // 2 for g in range(GCOLS)]

    HOT = 6
    hot = sorted(sorted(range(n_tables), key=lambda f: (tables[f].shape[0], -f))[:HOT])
    cold = [f for f in range(n_tables) if f not in hot]
    DUOS = HOT // 2
    VOCAB = tables[hot[0]].shape[0]
    CHUNKS = -(-VOCAB // P)
    VP = VOCAB // CHUNKS
    assert VP * CHUNKS == VOCAB and VOCAB <= 2048 and all(tables[f].shape[0] == VOCAB for f in hot)
    in_rows = [0] + [f + 1 for f in cold]
    ROW_BANKS = -(-len(in_rows) // FILL)

    TP = DUOS + HALVES * ROW_BANKS
    ROWS_AT = (2 * DUOS, 2 * DUOS + ROW_BANKS)
    IDS_AT = DUOS - TP
    GR = HALVES * GR_BANKS
    gathers = [[k for k in range(FILL * b, min(FILL * b + FILL, len(in_rows))) if k > 0] for b in range(ROW_BANKS)]
    GATHERED = [16 * len(group) for group in gathers]
    PT = COL_BANKS + PAIR_CHUNKS
    MM = N1 + N2 + 1
    RING = 4
    AHEAD = RING - 1
    STEPS = DUOS * CHUNKS
    assert HOT % 2 == 0 and UNITS * TP % 2 == 0 and GR % 2 == 0 and STEPS % RING == 0 and AHEAD < CHUNKS
    GROWS = (LANES - 1) * SLOT + feats - 1

    def plan(first, last, u):
        steps = []

        def some(of, n=1):
            for _ in range(min(n, len(of))):
                steps.append(of.pop(0))

        gram0, gram1 = ([("gram", h, k) for k in range(GR_BANKS)] for h in range(HALVES))
        rows0, rows1 = ([("rows", h, k) for k in range(ROW_BANKS)] for h in range(HALVES))
        columns = [("columns", k, 0) for k in range(COL_BANKS)]
        packed_pairs = [("pairs", c, 0) for c in range(PAIR_CHUNKS)]
        if last:
            with_x = [("open1", n, 0) for n in range(N1)]
            with_pairs = [("more1", n, c) for c in range(PAIR_CHUNKS) for n in range(N1)]
            some(gram0, GR_BANKS)
            some(rows1, ROW_BANKS)
            some(gram1, GR_BANKS)
            steps.append(("commit", 0, 0))
            some(columns, COL_BANKS - 2)
            for _ in range(2):
                some(with_x)
                some(columns)
            some(with_x)
            some(packed_pairs, 2)
            some(with_x)
            some(packed_pairs, 1)
            some(with_pairs, len(with_pairs))
            return steps + [("wide2", c, 0) for c in range(N1)] + [("layer3", 0, 0)]

        hots = [("hot", d, c) for d in range(DUOS) for c in range(CHUNKS)]
        ids_ = [("ids", d, 0) for d in range(DUOS)]
        mlp = [("layer1", n, 0) for n in range(N1)] + [("layer2", n, 0) for n in range(N2)] + [("layer3", 0, 0)]
        if first or u == 0:
            mlp = packed_pairs = []
        if first or u == 1:
            columns = []
        if first and u == 0:
            gram0 = gram1 = rows1 = []

        steps.append(("lead", 0, 0))
        for s in range(GR_BANKS):
            some(packed_pairs)
            some(hots, -(-(len(hots) - ROW_BANKS) // (GR_BANKS - s)))
            some(gram0)
            if s % 2 == 1 and not packed_pairs:
                some(mlp)
        for s in range(ROW_BANKS):
            some(rows1)
            some(hots)
        some(ids_)
        for s in range(GR_BANKS):
            some(gram1)
            if s == 0 and u == 0 and not first:
                steps.append(("commit", 0, 0))
            some(ids_)
            if s % 2 == 1:
                some(mlp)
            if u == 1 and not first and s >= 2:
                some(rows0)
        if first and u == 1:
            steps.append(("split_w1", 0, 0))
        while columns:
            some(rows0)
            some(columns)
        some(rows0, len(rows0))
        assert not (hots or mlp or packed_pairs or ids_ or gram0 or gram1 or rows1)
        return steps

    def runs(features):
        found, at = [], 0
        while at < len(features):
            n = 1
            while at + n < len(features) and features[at + n] - features[at + n - 1] == features[at + min(1, n)] - features[at]:
                n += 1
            found.append((at, features[at], features[at + 1] - features[at] if n > 1 else 1, n))
            at += n
        return found

    with ExitStack() as ctx:
        def sb(name, shape, dt=F32):
            return ctx.enter_context(nc.sbuf_tensor(name, shape, dt))

        def banks(name):
            return [ctx.enter_context(nc.psum_tensor(f"{name}{s}", [P, 512], F32)) for s in range(2)]

        def sem(name):
            return ctx.enter_context(nc.semaphore(name))

        index_both = sb("index", [P, HALVES, n_tables], I32)
        index = [index_both[:, s, :] for s in range(HALVES)]
        hot_all = sb("hot_all", [P, batch // P + 2 * HALVES, HOT], F16)
        hot_ids = [sb(f"hot_ids{s}", [P, HALVES, HOT], F16) for s in range(UNITS)]
        ids_cols = sb("ids_cols", [P, DUOS, 2 * UNIT], F16)
        onehot = sb("onehot", [P, RING, 2 * UNIT], F32R)
        high = sb("high", [P, HOT, CHUNKS, P], F32R)
        low = sb("low", [P, HOT, CHUNKS, P], F32R)
        rows = [sb(f"rows{s}", [P, len(in_rows), P]) for s in range(HALVES)]
        feat = sb("feat", [P, TILES, P, SLOT])
        x_high = sb("x_high", [P, BLOCK], F32R)
        x_low = sb("x_low", [P, BLOCK], F32R)
        gram = sb("gram", [P, GCOLS, P])
        packed = sb("packed", [P, LANES, pairs])
        pair_high = sb("pair_high", [P, PAIR_CHUNKS, BLOCK], F32R)
        pair_low = sb("pair_low", [P, PAIR_CHUNKS, BLOCK], F32R)
        h1 = sb("h1", [P, N1, BLOCK])
        h2 = packed[:].rearrange("q j p -> q (j p)")[:, 0:N2 * BLOCK].rearrange("p (c b) -> p c b", c=N2)
        w1x_high = sb("w1x_high", [P, hidden1], F32R)
        w1x_low = sb("w1x_low", [P, hidden1], F32R)
        w1p_high = sb("w1p_high", [P, PAIR_CHUNKS, hidden1], F32R)
        w1p_low = sb("w1p_low", [P, PAIR_CHUNKS, hidden1], F32R)
        w2 = sb("w2", [P, N1, hidden2])
        y = h1[0:1, 0, :]
        small = sb("small", [P, N2 + N1 + N2 + CHUNKS])
        w3, b1, b2 = small[:, 0:N2], small[:, N2:N2 + N1], small[:, N2 + N1:2 * N2 + N1]
        row_of = small[:, 2 * N2 + N1:]
        ident = sb("ident", [P, P])
        ident16 = sb("ident16", [P, P], F16)
        raw = [h1[:, 2 * s:2 * s + 2, :].rearrange("p n b -> p (n b)").rearrange("p (c d) -> p c d", d=P)
               for s in range(2)]
        w1p = h1[:, 0:PAIR_CHUNKS, 0:hidden1]
        spare = packed[:].rearrange("q j p -> q (j p)")
        all_index = spare[:, 0:batch // P * n_tables].bitcast(I32).rearrange("p (t f) -> p t f", f=n_tables)
        row_of_int = spare[:, batch // P * n_tables:batch // P * n_tables + CHUNKS].bitcast(I32)
        w1x, w1x_again = spare[:, 0:hidden1], spare[:, hidden1:2 * hidden1]

        tp = banks("tp")
        ht = banks("ht")
        gr = banks("gr")
        cm = banks("cm")
        wide = tp + ht

        weights_landed = sem("weights_landed")
        raw_landed = [sem(f"raw_landed{s}") for s in range(2)]
        high_ready = sem("high_ready")
        low_ready = sem("low_ready")
        w1x_summed = sem("w1x_summed")
        w1_ready = sem("w1_ready")
        ident16_ready = sem("ident16_ready")
        ident_zeroed = sem("ident_zeroed")
        ident_ready = sem("ident_ready")
        row_of_made = sem("row_of_made")
        row_of_ready = sem("row_of_ready")
        feat_padded = sem("feat_padded")
        index_landed = [sem(f"index_landed{s}") for s in range(HALVES)]
        all_index_landed = sem("all_index_landed")
        hot_all_ready = sem("hot_all_ready")
        pair_high_ready = sem("pair_high_ready")
        w1_landed = sem("w1_landed")
        w1_high_ready = sem("w1_high_ready")
        x_high_ready = sem("x_high_ready")
        x_landed = [sem(f"x_landed{s}") for s in range(HALVES)]
        rows_landed = [[sem(f"rows_landed{s}_{k}") for k in range(ROW_BANKS)] for s in range(HALVES)]
        hot_ids_ready = sem("hot_ids_ready")
        tp_full = sem("tp_full")
        tp_taken = sem("tp_taken")
        onehot_ready = sem("onehot_ready")
        onehot_used = sem("onehot_used")
        ht_taken = sem("ht_taken")
        gr_full = sem("gr_full")
        gr0_taken = sem("gr0_taken")
        gr1_taken = sem("gr1_taken")
        pt_full = sem("pt_full")
        pt_taken = sem("pt_taken")
        mm_full = sem("mm_full")
        mm_taken = sem("mm_taken")
        tile_begun = sem("tile_begun")
        x_committed = sem("x_committed")
        y_stored = sem("y_stored")
        WEIGHTS = 16 * 4
        W1 = 16 * 3

        block = ctx.enter_context(nc.Block())

        def peeled(eng, body):
            body(0)
            with eng.Fori(1, BLOCKS) as i:
                body(i)
            body(BLOCKS)

        def first(i):
            return isinstance(i, int) and i == 0

        def last(i):
            return isinstance(i, int) and i == BLOCKS

        @block.sync
        def _(sp):
            def load_unit(i, u):
                n = UNITS * i + u
                start = i * BLOCK + u * UNIT
                for h in range(HALVES):
                    if not (first(i) and u == 0):
                        sp.wait_ge(tp_full, TP * (n - 1) + ROWS_AT[h] + ROW_BANKS)
                    sp.dma_start(index[h], ids[bass.ds(start + h * P, P), :]).then_inc(index_landed[h], 16)
                    sp.dma_start(rows[h][:, 0, :], x[bass.ds(start + h * P, P), :]).then_inc(x_landed[h], 16)

            def load_raw(t):
                s = t % 2
                if t >= 2:
                    sp.wait_ge(low_ready, t - 1)
                sp.dma_start(raw[s][0:VP], tables[hot[t]].rearrange("(p c) d -> p c d", c=CHUNKS)) \
                    .then_inc(raw_landed[s], 16)

            def load_w1():
                sp.wait_ge(low_ready, HOT)
                sp.dma_start(w1p[0:PCH], w_top1[P:P + pairs, :].rearrange("(c p) n -> p c n", p=PCH)) \
                    .then_inc(w1_landed, 16)
                sp.wait_ge(hot_all_ready, 1)
                sp.dma_start(w1x, w_top1[0:P, :]).then_inc(w1_landed, 16)
                sp.dma_start(w1x_again, w_top1[P + pairs:2 * P + pairs, :]).then_inc(w1_landed, 16)

            def load_weights():
                sp.dma_start(w2[:], w_top2.rearrange("(c p) n -> p c n", p=P)).then_inc(weights_landed, 16)
                with nc.allow_non_contiguous_dma(reason="a few hundred words, once"):
                    sp.dma_start(w3, w_top3.rearrange("(c p) o -> p (c o)", p=P)).then_inc(weights_landed, 16)
                    sp.dma_start(b1, b_top1.rearrange("(c p) -> p c", p=P)).then_inc(weights_landed, 16)
                    sp.dma_start(b2, b_top2.rearrange("(c p) -> p c", p=P)).then_inc(weights_landed, 16)

            def body(i):
                if last(i):
                    return
                for u in range(UNITS):
                    load_unit(i, u)
                    if first(i) and u == 0:
                        for t in range(HOT):
                            load_raw(t)
                            if t == 1:
                                load_weights()
                        load_w1()

            peeled(sp, body)

        @block.gpsimd
        def _(pool):
            def constants():
                nc.gpsimd.memset(ident[:], 0.0).then_inc(ident_zeroed, 1)
                pool.wait_ge(ident_zeroed, 1)
                nc.gpsimd.affine_select(out=ident[:], in_=ident[:], compare_op=ALU.not_equal, fill=1.0, base=0,
                                        pattern=[[-1, P]], channel_multiplier=1).then_inc(ident_ready, 1)
                nc.gpsimd.iota(row_of_int, pattern=[[1, CHUNKS]], base=0, channel_multiplier=CHUNKS) \
                    .then_inc(row_of_made, 1)

            def body(i):
                if first(i):
                    constants()
                if last(i):
                    return
                for u in range(UNITS):
                    n = UNITS * i + u
                    for h in range(HALVES):
                        pool.wait_ge(index_landed[h], 16 * (n + 1))
                        if not (first(i) and u == 0):
                            pool.wait_ge(tp_full, TP * (n - 1) + ROWS_AT[h] + ROW_BANKS)
                        pool.sem_inc(tile_begun, 1)
                        for landed, group in zip(rows_landed[h], gathers):
                            for k in group:
                                f = cold[k - 1]
                                nc.gpsimd.indirect_dma_start(
                                    rows[h][:, k, :], None, tables[f][:, :],
                                    bass.IndirectOffsetOnAxis(ap=index[h][:, f:f + 1], axis=0)) \
                                    .then_inc(landed, 16)

            peeled(pool, body)

        @block.tensor
        def _(pe):
            def tp_bank(i, u, k):
                if not (first(i) and TP * u + k < 2):
                    pe.wait_ge(tp_taken, TP * (UNITS * i + u) + k - 1)
                return tp[(TP * u + k) % 2]

            def spread_ids(i, u, k, d):
                to = tp_bank(i, u, k)
                for e in range(2):
                    for h in range(HALVES):
                        at = (e * HALVES + h) * P
                        t = 2 * d + e
                        ins = nc.tensor.matmul(to[:, at:at + P], hot_ids[(u + (k >= DUOS)) % UNITS][:, h, t:t + 1].to_broadcast([P, P]),
                                               ident16[:], start=True, stop=True)
                ins.then_inc(tp_full, 1)

            def turn_rows(i, u, h, k):
                n = UNITS * i + u
                if k == 0:
                    pe.wait_ge(x_landed[h], 16 * (n + 1))
                pe.wait_ge(rows_landed[h][k], GATHERED[k] * (n + 1))
                to = tp_bank(i, u, ROWS_AT[h] + k)
                for r in range(FILL * k, min(FILL * k + FILL, len(in_rows))):
                    at = (r - FILL * k) * P
                    ins = nc.tensor.transpose(to[:, at:at + P], rows[h][:, r, :], ident[:])
                ins.then_inc(tp_full, 1)

            def look_up(i, u, d, c):
                n = UNITS * i + u
                if c == 0 and not (first(i) and u == 0 and d < 2):
                    pe.wait_ge(ht_taken, DUOS * n + d - 1)
                if c == 0 and first(i) and u == 0:
                    pe.wait_ge(low_ready, 2 * d + 2)
                pe.wait_ge(onehot_ready, STEPS * n + CHUNKS * d + c + 1)
                for e in range(2):
                    t = 2 * d + e
                    to = ht[(DUOS * u + d) % 2][:, e * UNIT:(e + 1) * UNIT]
                    moving = onehot[0:VP, (CHUNKS * d + c) % RING, e * UNIT:(e + 1) * UNIT]
                    nc.tensor.matmul(to, high[0:VP, t, c, :], moving, start=(c == 0 and e == 0), stop=False,
                                     skip_group_check=True)
                    ins = nc.tensor.matmul(to, low[0:VP, t, c, :], moving, start=False, stop=(c == CHUNKS - 1),
                                           skip_group_check=True)
                ins.then_inc(onehot_used, 1)

            def gram_bank(i, u, h, k):
                n = UNITS * i + u
                if k == 0:
                    pe.wait_ge(tp_taken, TP * n + ROWS_AT[h] + ROW_BANKS)
                    if h == 0:
                        pe.wait_ge(ht_taken, DUOS * (n + 1))
                m = GR * n + GR_BANKS * h + k
                if not (first(i) and u == 0 and h == 0 and k < 2):
                    pe.wait_ge((gr0_taken, gr1_taken)[k % 2], GR // 2 * n + (GR_BANKS * h + k) // 2)
                for q in range(FILL):
                    b = LANES * (FILL * k + q)
                    items = feat[:, HALVES * u + h, b:b + LANES, :]
                    ins = nc.tensor.matmul(gr[k % 2][0:GROWS, q * LANES * GCOLS:(q + 1) * LANES * GCOLS],
                                           items.rearrange("d j f -> d (j f)")[:, 1:1 + GROWS],
                                           items[:, :, 0:GCOLS], start=True, stop=True)
                ins.then_inc(gr_full, 1)

            def turn_columns(i, k):
                if k == 0:
                    pe.wait_ge(gr0_taken, GR // 2 * UNITS * (i + 1))
                    pe.wait_ge(gr1_taken, GR // 2 * UNITS * (i + 1))
                if k >= 2:
                    pe.wait_ge(pt_taken, PT * i + k - 1)
                for g in range(FILL * k, min(FILL * k + FILL, GCOLS)):
                    at = (g - FILL * k) * P
                    ins = nc.tensor.transpose(cm[k % 2][:, at:at + GROWS], gram[0:GROWS, g, :],
                                              ident[0:GROWS, 0:GROWS])
                ins.then_inc(pt_full, 1)

            def turn_pairs(i, c):
                k = COL_BANKS + c
                if c == 0:
                    pe.wait_ge(pt_taken, PT * i + COL_BANKS)
                else:
                    pe.wait_ge(pt_taken, PT * i + k - 1)
                for j in range(LANES):
                    ins = nc.tensor.transpose(cm[k % 2][0:PCH, j * P:(j + 1) * P],
                                              packed[:, j, c * PCH:(c + 1) * PCH], ident[:])
                ins.then_inc(pt_full, 1)

            def mm_bank(i, k):
                if k == 0:
                    pe.wait_ge(pt_taken, PT * (i + 1) - 1)
                elif k >= 2:
                    pe.wait_ge(mm_taken, MM * i + k - 1)
                return cm[(PT + k) % 2]

            def layer1(i, n):
                to = mm_bank(i, n)
                if n == 0:
                    pe.wait_ge(x_committed, i + 1)
                    pe.wait_ge(w1_ready, 2)
                    pe.wait_ge(weights_landed, WEIGHTS)
                cols = slice(n * P, (n + 1) * P)
                parts = [(w1x_high[:, cols], w1x_low[:, cols], x_high[:], x_low[:])]
                parts += [(w1p_high[0:PCH, c, cols], w1p_low[0:PCH, c, cols], pair_high[0:PCH, c, :],
                           pair_low[0:PCH, c, :]) for c in range(PAIR_CHUNKS)]
                for c, (w_high, w_low, high_, low_) in enumerate(parts):
                    if n == 0 and c == 1:
                        pe.wait_ge(pt_taken, PT * (i + 1))
                    nc.tensor.matmul(to[:], w_high, high_, start=(c == 0), stop=False)
                    nc.tensor.matmul(to[:], w_high, low_, start=False, stop=False)
                    ins = nc.tensor.matmul(to[:], w_low, high_, start=False, stop=(c == PAIR_CHUNKS))
                ins.then_inc(mm_full, 1)

            def layer1_part(i, n, part):
                if n == 0:
                    if part == 0:
                        pe.wait_ge(x_committed, i + 1)
                    else:
                        pe.wait_ge(pt_taken, PT * i + COL_BANKS + part)
                to, cols = wide[n], slice(n * P, (n + 1) * P)
                if part == 0:
                    w_high, w_low, high_, low_ = w1x_high[:, cols], w1x_low[:, cols], x_high[:], x_low[:]
                else:
                    w_high, w_low = w1p_high[0:PCH, part - 1, cols], w1p_low[0:PCH, part - 1, cols]
                    high_, low_ = pair_high[0:PCH, part - 1, :], pair_low[0:PCH, part - 1, :]
                nc.tensor.matmul(to[:], w_high, high_, start=(part == 0), stop=False)
                nc.tensor.matmul(to[:], w_high, low_, start=False, stop=False)
                ins = nc.tensor.matmul(to[:], w_low, high_, start=False, stop=(part == PAIR_CHUNKS))
                if part == PAIR_CHUNKS:
                    ins.then_inc(mm_full, 1)

            def layer2_wide(i, c):
                pe.wait_ge(mm_taken, MM * i + c + 1)
                for n in range(N2):
                    ins = nc.tensor.matmul(gr[n][:], w2[:, c, n * P:(n + 1) * P], h1[:, c, :],
                                           start=(c == 0), stop=(c == N1 - 1))
                    if c == N1 - 1:
                        ins.then_inc(mm_full, 1)

            def layer2(i, n):
                to = mm_bank(i, N1 + n)
                if n == 0:
                    pe.wait_ge(mm_taken, MM * i + N1)
                for c in range(N1):
                    ins = nc.tensor.matmul(to[:], w2[:, c, n * P:(n + 1) * P], h1[:, c, :],
                                           start=(c == 0), stop=(c == N1 - 1))
                ins.then_inc(mm_full, 1)

            def layer3(i):
                to = mm_bank(i, N1 + N2)
                for c in range(N2):
                    pe.wait_ge(mm_taken, MM * i + N1 + c + 1)
                    ins = nc.tensor.matmul(to[0:1, :], w3[:, c:c + 1], h2[:, c, :], start=(c == 0), stop=(c == N2 - 1))
                ins.then_inc(mm_full, 1)

            def body(i):
                if first(i):
                    pe.wait_ge(ident_ready, 1)
                    pe.wait_ge(ident16_ready, 1)
                    pe.wait_ge(feat_padded, 1)
                    pe.wait_ge(hot_ids_ready, 1)
                    for d in range(DUOS):
                        spread_ids(0, 0, d, d)
                for u in range(1 if last(i) else UNITS):
                    for what, a, b in plan(first(i), last(i), u):
                        if what == "ids":
                            if a == 0:
                                pe.wait_ge(hot_ids_ready, UNITS * i + u + 2)
                            spread_ids(i, u, DUOS + a, a)
                        elif what == "rows":
                            if a == 0:
                                turn_rows(i, u, a, b)
                            else:
                                turn_rows(i - (u == 0), (u + 1) % UNITS, a, b)
                        elif what == "hot":
                            look_up(i, u, a, b)
                        elif what == "gram":
                            gram_bank(i - (u == 0), (u + 1) % UNITS, a, b)
                        elif what == "columns":
                            turn_columns(i - 1, a)
                        elif what == "pairs":
                            turn_pairs(i - 1, a)
                        elif what == "layer1":
                            layer1(i - 1, a)
                        elif what == "open1":
                            layer1_part(i - 1, a, 0)
                        elif what == "more1":
                            layer1_part(i - 1, a, b + 1)
                        elif what == "layer2":
                            layer2(i - 1, a)
                        elif what == "wide2":
                            layer2_wide(i - 1, a)
                        elif what == "layer3":
                            layer3(i - 1)

            peeled(pe, body)

        @block.scalar
        def _(act):
            def pick_ids(n, u):
                nc.scalar.copy(hot_ids[u][:], hot_all[:, bass.ds(HALVES * n, HALVES), :]).then_inc(hot_ids_ready, 1)

            def take_high(d):
                for t in (2 * d, 2 * d + 1):
                    act.wait_ge(raw_landed[t % 2], 16 * (t // 2 + 1))
                    nc.scalar.copy(high[0:VP, t], raw[t % 2][0:VP]).then_inc(high_ready, 1)

            def take_ids(i, u, k, d):
                n = UNITS * i + u
                act.wait_ge(tp_full, TP * n + k + 1)
                if d == 0 and k >= DUOS:
                    act.wait_ge(onehot_ready, STEPS * (n + 1))
                nc.scalar.copy(ids_cols[:, d, :], tp[(TP * u + k) % 2][:]).then_inc(tp_taken, 1)

            def take_rows(i, u, h, k):
                n = UNITS * i + u
                m = ROWS_AT[h] + k
                t = HALVES * u + h
                features = in_rows[FILL * k:FILL * k + FILL]
                act.wait_ge(tp_full, TP * n + m + 1)
                src = tp[(TP * u + m) % 2]
                if k == 0:
                    if t == 0 and not first(i):
                        act.wait_ge(x_committed, i)
                    if h == 0 and not first(i):
                        act.wait_ge(gr_full, GR * (n - 1))
                for at, f, step, count in runs(features):
                    to = feat[:, t, :, f:f + step * (count - 1) + 1:step]
                    ins = nc.scalar.copy(to.rearrange("d b f -> d f b"),
                                         src[:, at * P:(at + count) * P].rearrange("d (f b) -> d f b", b=P))
                ins.then_inc(tp_taken, 1)

            def take_looked_up(i, u, d):
                n = UNITS * i + u
                act.wait_ge(onehot_used, STEPS * n + CHUNKS * (d + 1))
                if d == 0 and not first(i):
                    act.wait_ge(gr_full, GR * (n - 1))
                a, b = hot[2 * d] + 1, hot[2 * d + 1] + 1
                for h in range(HALVES):
                    ins = nc.scalar.copy(feat[:, HALVES * u + h, :, a:b + 1:b - a].rearrange("d b e -> d e b"),
                                         ht[(DUOS * u + d) % 2][:].rearrange("d (e h b) -> d e h b", e=2, h=HALVES)
                                         [:, :, h, :])
                ins.then_inc(ht_taken, 1)

            def take_gram(i, u, h, k):
                act.wait_ge(gr_full, GR * (UNITS * i + u) + GR_BANKS * h + k + 1)
                quad = (HALVES * u + h) * QUADS + FILL * k
                for j in range(LANES):
                    part = slice(j * SLOT, j * SLOT + feats - 1)
                    src = gr[k % 2][part, 0:FILL * LANES * GCOLS].rearrange("p (q j g) -> p q j g", q=FILL, j=LANES)
                    ins = nc.scalar.copy(gram[part, :, quad:quad + FILL].rearrange("p g q -> p q g"), src[:, :, j, :])
                ins.then_inc(gr1_taken, 1)

            def take_pairs_high(i, c):
                k = COL_BANKS + c
                act.wait_ge(pt_full, PT * i + k + 1)
                nc.scalar.copy(pair_high[0:PCH, c, :], cm[k % 2][0:PCH, :]).then_inc(pair_high_ready, 1)

            def split_w1_high():
                act.wait_ge(w1_landed, W1)
                nc.scalar.copy(w1p_high[0:PCH], w1p[0:PCH]).then_inc(w1_high_ready, 1)
                act.wait_ge(w1x_summed, 1)
                nc.scalar.copy(w1x_high[:], w1x).then_inc(w1_high_ready, 1)

            def relu(i, k, to, bias, bank=None):
                act.wait_ge(mm_full, MM * i + k + 1)
                nc.scalar.activation(to, (bank or cm[(PT + k) % 2])[:], ACT.Relu, bias=bias).then_inc(mm_taken, 1)

            def give_y(i):
                act.wait_ge(mm_full, MM * (i + 1))
                nc.scalar.copy(y.rearrange("o (q j) -> o j q", j=LANES),
                               cm[(PT + N1 + N2) % 2][0:1, :].rearrange("o (j q) -> o j q", j=LANES)).then_inc(mm_taken, 1)
                act.wait_ge(mm_taken, MM * (i + 1))
                act.dma_start(out[bass.ds(i * BLOCK, BLOCK), :].rearrange("b o -> o b"), y).then_inc(y_stored, 16)

            def body(i):
                if first(i):
                    act.dma_start(all_index, ids.rearrange("(t p) f -> p t f", p=P)).then_inc(all_index_landed, 16)
                    act.wait_ge(hot_all_ready, 1)
                    for u in range(UNITS):
                        pick_ids(u, u)
                    take_high(0)
                    for d in range(DUOS):
                        take_ids(0, 0, d, d)
                for u in range(1 if last(i) else UNITS):
                    for what, a, b in plan(first(i), last(i), u):
                        if what == "ids":
                            take_ids(i, u, DUOS + a, a)
                            if a == DUOS - 1:
                                pick_ids(UNITS * i + u + 2, u)
                        elif what == "rows":
                            if a == 0:
                                take_rows(i, u, a, b)
                            else:
                                take_rows(i - (u == 0), (u + 1) % UNITS, a, b)
                        elif what == "hot" and b == 0 and first(i) and u == 0 and a + 1 < DUOS:
                            take_high(a + 1)
                        elif what == "hot" and b == CHUNKS - 1:
                            take_looked_up(i, u, a)
                        elif what == "gram" and b % 2 == 1:
                            take_gram(i - (u == 0), (u + 1) % UNITS, a, b)
                        elif what == "split_w1":
                            split_w1_high()
                        elif what == "pairs":
                            take_pairs_high(i - 1, a)
                        elif what == "layer1":
                            relu(i - 1, a, h1[:, a, :], b1[:, a:a + 1])
                        elif what == "more1" and b == PAIR_CHUNKS - 1:
                            relu(i - 1, a, h1[:, a, :], b1[:, a:a + 1], wide[a])
                        elif what == "wide2" and a == N1 - 1:
                            for n in range(N2):
                                relu(i - 1, N1 + n, h2[:, n, :], b2[:, n:n + 1], gr[n])
                        elif what == "layer2":
                            relu(i - 1, N1 + a, h2[:, a, :], b2[:, a:a + 1])
                        elif what == "layer3":
                            give_y(i - 1)
                    if (u == UNITS - 1 or last(i)) and not first(i):
                        act.wait_ge(y_stored, 16 * i)

            peeled(act, body)

        @block.vector
        def _(dve):
            def take_low(d):
                for t in (2 * d, 2 * d + 1):
                    dve.wait_ge(high_ready, t + 1)
                    nc.vector.tensor_tensor(low[0:VP, t], raw[t % 2][0:VP], high[0:VP, t].bitcast(F32),
                                            ALU.subtract).then_inc(low_ready, 1)

            def split_w1():
                dve.wait_ge(w1_landed, W1)
                nc.vector.tensor_tensor(w1x, w1x, w1x_again, ALU.add).then_inc(w1x_summed, 1)
                dve.wait_ge(w1_high_ready, 1)
                nc.vector.tensor_tensor(w1p_low[0:PCH], w1p[0:PCH], w1p_high[0:PCH].bitcast(F32),
                                        ALU.subtract).then_inc(w1_ready, 1)
                dve.wait_ge(w1_high_ready, 2)
                nc.vector.tensor_tensor(w1x_low[:], w1x, w1x_high[:].bitcast(F32), ALU.subtract).then_inc(w1_ready, 1)

            def make_onehot(i, u, m):
                n = UNITS * i + u
                d, c = divmod(m, CHUNKS)
                if c == 0:
                    if first(i) and u == 0:
                        dve.wait_ge(tp_taken, d + 1)
                    else:
                        dve.wait_ge(tp_taken, TP * n + IDS_AT + d + 1)
                if not (first(i) and u == 0 and m < RING):
                    dve.wait_ge(onehot_used, STEPS * n + m - RING + 1)
                nc.vector.tensor_scalar(onehot[0:VP, m % RING, :], ids_cols[0:VP, d, :], row_of[0:VP, c:c + 1], None,
                                        ALU.is_equal).then_inc(onehot_ready, 1)

            def take_gram(i, u, h, k):
                dve.wait_ge(gr_full, GR * (UNITS * i + u) + GR_BANKS * h + k + 1)
                quad = (HALVES * u + h) * QUADS + FILL * k
                for j in range(LANES):
                    part = slice(j * SLOT, j * SLOT + feats - 1)
                    src = gr[k % 2][part, 0:FILL * LANES * GCOLS].rearrange("p (q j g) -> p q j g", q=FILL, j=LANES)
                    ins = nc.vector.tensor_copy(gram[part, :, quad:quad + FILL].rearrange("p g q -> p q g"),
                                                src[:, :, j, :])
                ins.then_inc(gr0_taken, 1)

            def commit_x(i):
                dve.wait_ge(tp_taken, TP * (UNITS * i - 1) + ROWS_AT[1] + 1)
                block_x = feat[:, :, :, 0].rearrange("d t (q j) -> d t q j", j=LANES)
                high_, low_ = (part[:].rearrange("d (j t q) -> d t q j", j=LANES, t=TILES) for part in (x_high, x_low))
                nc.vector.tensor_copy(high_, block_x).then_inc(x_high_ready, 1)
                dve.wait_ge(x_high_ready, i)
                nc.vector.tensor_tensor(low_, block_x, high_.bitcast(F32), ALU.subtract).then_inc(x_committed, 1)

            def take_columns(i, k):
                dve.wait_ge(pt_full, PT * i + k + 1)
                for g in range(FILL * k, min(FILL * k + FILL, GCOLS)):
                    at = (g - FILL * k) * P
                    src = cm[k % 2][:, at:at + P].rearrange("q (j f) -> q j f", j=LANES)
                    ins = nc.vector.tensor_copy(packed[:, :, pair_at[g]:pair_at[g] + feats - 1 - g],
                                                src[:, :, g:feats - 1])
                ins.then_inc(pt_taken, 1)

            def take_pairs(i, c):
                k = COL_BANKS + c
                dve.wait_ge(pt_full, PT * i + k + 1)
                dve.wait_ge(pair_high_ready, PAIR_CHUNKS * i + c + 1)
                nc.vector.tensor_tensor(pair_low[0:PCH, c, :], cm[k % 2][0:PCH, :], pair_high[0:PCH, c, :].bitcast(F32),
                                        ALU.subtract).then_inc(pt_taken, 1)

            def body(i):
                if first(i):
                    nc.vector.memset(feat[:, :, :, feats:SLOT], 0.0).then_inc(feat_padded, 1)
                    dve.wait_ge(row_of_made, 1)
                    nc.vector.tensor_copy(row_of, row_of_int).then_inc(row_of_ready, 1)
                    dve.wait_ge(row_of_ready, 1)
                    dve.wait_ge(ident_ready, 1)
                    nc.vector.tensor_copy(ident16[:], ident[:]).then_inc(ident16_ready, 1)
                    nc.vector.memset(hot_all[:, batch // P:, :], 0.0)
                    dve.wait_ge(all_index_landed, 16)
                    for at, f, step, count in runs(hot):
                        ins = nc.vector.tensor_copy(hot_all[:, 0:batch // P, at:at + count],
                                                    all_index[:, :, f:f + step * (count - 1) + 1:step])
                    ins.then_inc(hot_all_ready, 1)
                    take_low(0)
                for u in range(1 if last(i) else UNITS):
                    for what, a, b in plan(first(i), last(i), u):
                        if what == "lead" and not last(i):
                            for m in range(AHEAD):
                                make_onehot(i, u, m)
                        elif what == "hot":
                            m = CHUNKS * a + b
                            if first(i) and u == 0 and b == CHUNKS // 2 and a + 1 < DUOS:
                                take_low(a + 1)
                            if m + AHEAD < STEPS:
                                make_onehot(i, u, m + AHEAD)
                        elif what == "gram" and b % 2 == 0:
                            take_gram(i - (u == 0), (u + 1) % UNITS, a, b)
                        elif what == "columns":
                            take_columns(i - 1, a)
                        elif what == "pairs":
                            take_pairs(i - 1, a)
                        elif what == "commit":
                            commit_x(i)
                        elif what == "split_w1":
                            split_w1()

            peeled(dve, body)


def kernel(**inputs):
    import numpy as _np
    import concourse.bacc as _bacc
    from concourse import mybir as _mybir
    from concourse.bass_utils import run_bass_kernel_spmd as _run

    nc = _bacc.Bacc("TRN2", target_bir_lowering=False, num_devices=1)
    arrays, dram = {}, {}
    for name, value in inputs.items():
        a = _np.ascontiguousarray(value)
        arrays[f"in_{name}"] = a
        dram[name] = nc.dram_tensor(f"in_{name}", a.shape, _mybir.dt.from_np(a.dtype), kind="ExternalInput").ap()
    tables = [dram[f"tbl_{n}"] for n in range(dram["ids"].shape[1])]
    batch = dram["ids"].shape[0]
    out = nc.dram_tensor("out_y", (batch, 1), _mybir.dt.float32, kind="ExternalOutput").ap()
    dlrm_tower(nc, dram["r_dense_features"], dram["ids"], tables, dram["W_top1"], dram["b_top1"],
               dram["W_top2"], dram["b_top2"], dram["W_top3"], out)
    r = _run(nc, [arrays], core_ids=[0])
    return r.results[0]["out_y"]
```
